# Optimizing a Trainium2 kernel written in Bass

```python
import numpy as np
import jax
import jax.numpy as jnp

def _softmax(x, axis=-1):
    return jax.nn.softmax(x, axis=axis)

def _gelu(x):
    return jax.nn.gelu(x, approximate=True)

def _silu(x):
    return jax.nn.silu(x)

def _sigmoid(x):
    return jax.nn.sigmoid(x)

def _layernorm(x, axis=-1, eps=1e-05):
    m = jnp.mean(x, axis=axis, keepdims=True)
    v = jnp.var(x, axis=axis, keepdims=True)
    return (x - m) / jnp.sqrt(v + eps)

def _scatter_add(tgt, idx, src, axis=0):
    return tgt.at[idx].add(src)

def _segment_sum(src, seg, n):
    return jax.ops.segment_sum(src, seg, n)
kernel_name = 'mk_seq_preln_d1_jaxref_r4_5cbb7b'

def setup_inputs(seed: int=0):
    np.random.seed(seed)
    _w = jnp.asarray

    def _L0_attn_setup():
        import jax, jax.numpy as jnp
        import numpy as np
        B, S, E = (2, 1024, 256)
        H = 16
        W = 64

        def _chunk3(x):
            prev = jnp.pad(x[:, :-1], ((0, 0), (1, 0), (0, 0), (0, 0), (0, 0)))
            nxt = jnp.pad(x[:, 1:], ((0, 0), (0, 1), (0, 0), (0, 0), (0, 0)))
            return jnp.stack([prev, x, nxt], axis=-1)
        key = jax.random.key(seed)
        ks = jax.random.split(key, 4)
        hs = jax.random.normal(ks[0], (B, S, E), jnp.float32)

        def lin(k):
            kw, kb = jax.random.split(k)
            return (jax.random.normal(kw, (E, E), jnp.float32) * 0.02, jax.random.normal(kb, (E,), jnp.float32) * 0.02)
        Wq, bq = lin(ks[1])
        Wk, bk = lin(ks[2])
        Wv, bv = lin(ks[3])
        return {'hidden_states': hs, 'Wq': Wq, 'bq': bq, 'Wk': Wk, 'bk': bk, 'Wv': Wv, 'bv': bv}
    _L0_attn_in = _L0_attn_setup()

    def _L0_ffn_setup():
        import jax, jax.numpy as jnp
        import numpy as np
        D = 256
        H = 1024
        E = 8
        TOPK = 2
        CAP_F = 1.25
        key = jax.random.key(seed)
        ks = jax.random.split(key, 6)
        sc = 0.02
        return {'x': jax.random.normal(ks[0], (4, 512, D), jnp.float32), 'Wg': jax.random.normal(ks[1], (D, E), jnp.float32) * sc, 'bg': jnp.zeros((E,), jnp.float32), 'W1': jax.random.normal(ks[2], (E, D, H), jnp.float32) * sc, 'W2': jax.random.normal(ks[3], (E, D, H), jnp.float32) * sc, 'W3': jax.random.normal(ks[4], (E, H, D), jnp.float32) * sc}
    _L0_ffn_in = _L0_ffn_setup()
    _d = {'L0_attn_hidden_states': _L0_attn_in['hidden_states'], 'L0_attn_Wq': _L0_attn_in['Wq'], 'L0_attn_bq': _L0_attn_in['bq'], 'L0_attn_Wk': _L0_attn_in['Wk'], 'L0_attn_bk': _L0_attn_in['bk'], 'L0_attn_Wv': _L0_attn_in['Wv'], 'L0_attn_bv': _L0_attn_in['bv'], 'L0_ffn_Wg': _L0_ffn_in['Wg'], 'L0_ffn_bg': _L0_ffn_in['bg'], 'L0_ffn_W1': _L0_ffn_in['W1'], 'L0_ffn_W2': _L0_ffn_in['W2'], 'L0_ffn_W3': _L0_ffn_in['W3']}
    _x0 = _d['L0_attn_hidden_states']
    _d['L0_attn_hidden_states'] = jax.random.normal(jax.random.fold_in(jax.random.key(seed), 1), (32, 512, 256), dtype=_x0.dtype)
    del _x0
    return _d

def reference(L0_attn_hidden_states, L0_attn_Wq, L0_attn_bq, L0_attn_Wk, L0_attn_bk, L0_attn_Wv, L0_attn_bv, L0_ffn_Wg, L0_ffn_bg, L0_ffn_W1, L0_ffn_W2, L0_ffn_W3):

    def _L0_attn_ref(hidden_states, Wq, bq, Wk, bk, Wv, bv):
        import jax, jax.numpy as jnp
        import numpy as np
        B, S, E = (2, 1024, 256)
        H = 16
        W = 64

        def _chunk3(x):
            prev = jnp.pad(x[:, :-1], ((0, 0), (1, 0), (0, 0), (0, 0), (0, 0)))
            nxt = jnp.pad(x[:, 1:], ((0, 0), (0, 1), (0, 0), (0, 0), (0, 0)))
            return jnp.stack([prev, x, nxt], axis=-1)
        b, s, e = hidden_states.shape
        h, w = (H, W)
        d = e // h
        nc = s // w
        q = (hidden_states @ Wq.T + bq) * (1.0 / np.sqrt(d))
        k = hidden_states @ Wk.T + bk
        v = hidden_states @ Wv.T + bv
        q = q.reshape(b, s, h, d)
        k = k.reshape(b, s, h, d)
        v = v.reshape(b, s, h, d)
        cq = q.reshape(b, nc, w, h, d)
        ck3 = _chunk3(k.reshape(b, nc, w, h, d))
        scores = jnp.einsum('bcxhd,bcyhde->bcxhey', cq, ck3).reshape(b, s, h, 3 * w)
        ii = jnp.arange(w)[:, None]
        cc = jnp.arange(w + 1)[None, :]
        beg_mask = cc < w - ii
        end_mask = cc >= w - ii
        neg_inf = jnp.array(-jnp.inf, scores.dtype)
        beg = jnp.where(beg_mask[None, :, None, :], neg_inf, scores[:, :w, :, :w + 1])
        scores = scores.at[:, :w, :, :w + 1].set(beg)
        end = jnp.where(end_mask[None, :, None, :], neg_inf, scores[:, s - w:, :, 3 * w - (w + 1):])
        scores = scores.at[:, s - w:, :, 3 * w - (w + 1):].set(end)
        probs = jax.nn.softmax(scores.astype(jnp.float32), axis=-1).astype(hidden_states.dtype)
        cp = probs.reshape(b, nc, w, h, 3, w)
        cv3 = _chunk3(v.reshape(b, nc, w, h, d))
        attn = jnp.einsum('bcwhpd,bcdhep->bcwhe', cp, cv3).reshape(b, s, h, d)
        return attn.reshape(b, s, e)

    def _L0_ffn_ref(x, Wg, bg, W1, W2, W3):
        import jax, jax.numpy as jnp
        import numpy as np
        D = 256
        H = 1024
        E = 8
        TOPK = 2
        CAP_F = 1.25
        b, s, d = x.shape
        xt = x.reshape(-1, d)
        T = xt.shape[0]
        capacity = int(T / E * CAP_F)
        gate_logits = xt @ Wg + bg
        top_v, top_i = jax.lax.top_k(gate_logits, TOPK)
        expert_label = jax.nn.one_hot(top_i, E, dtype=xt.dtype).sum(axis=1)
        seq = jnp.cumsum(expert_label, axis=0) * expert_label
        valid = (seq > 0) & (seq <= capacity)
        slot = (seq - 1.0).astype(jnp.int32)
        flat_idx = jnp.where(valid, jnp.arange(E, dtype=jnp.int32)[None, :] * capacity + slot, E * capacity)
        src = jnp.broadcast_to(xt[:, None, :], (T, E, d)).reshape(-1, d)
        buf = jnp.zeros((E * capacity + 1, d), xt.dtype).at[flat_idx.reshape(-1)].set(src)
        disp = buf[:-1].reshape(E, capacity, d)
        h = jax.nn.silu(jnp.einsum('ecd,edh->ech', disp, W1)) * jnp.einsum('ecd,edh->ech', disp, W2)
        out = jnp.einsum('ech,ehd->ecd', h, W3)
        out_flat = jnp.concatenate([out.reshape(E * capacity, d), jnp.zeros((1, d), xt.dtype)], axis=0)
        all_expert_output = out_flat[flat_idx]
        sel = jnp.take_along_axis(all_expert_output, top_i[:, :, None], axis=1)
        routing_w = jax.nn.softmax(top_v, axis=-1)
        y = (routing_w[:, :, None] * sel).sum(axis=1)
        return y.reshape(b, s, d)
    x = L0_attn_hidden_states
    x = x + _L0_attn_ref(_layernorm(x, axis=-1), L0_attn_Wq, L0_attn_bq, L0_attn_Wk, L0_attn_bk, L0_attn_Wv, L0_attn_bv)
    x = x + _L0_ffn_ref(_layernorm(x, axis=-1), L0_ffn_Wg, L0_ffn_bg, L0_ffn_W1, L0_ffn_W2, L0_ffn_W3)
    return x

_drawn_inputs = setup_inputs


def setup_inputs(seed=0):
    import zlib

    import numpy as np

    out = dict(_drawn_inputs(seed))
    spreads = {'L0_ffn_bg': (0.0, 0.749)}
    factors = {'L0_attn_Wq': 8.0,
     'L0_attn_bq': 8.0,
     'L0_attn_Wk': 8.0,
     'L0_attn_bk': 200.0,
     'L0_attn_bv': 2.787,
     'L0_ffn_Wg': 3.457,
     'L0_ffn_W1': 3.033,
     'L0_ffn_W2': 3.0,
     'L0_ffn_W3': 2.999}
    for name, (base, spread) in spreads.items():
        noise = np.random.default_rng([zlib.crc32(name.encode()), seed]).standard_normal(out[name].shape)
        drawn = base * np.exp(spread * noise) if base else spread * noise
        out[name] = jnp.asarray(drawn.astype(out[name].dtype))
    for name, factor in factors.items():
        out[name] = (out[name] * factor).astype(out[name].dtype)
    return out
```

```python
from contextlib import ExitStack

import concourse.bass as bass
from concourse import mybir

F32 = mybir.dt.float32
F32R = mybir.dt.float32r
U32 = mybir.dt.uint32
ALU = mybir.AluOpType
ACT = mybir.ActivationFunctionType
AX = mybir.AxisListType

P = 128
NB, S, E = 32, 512, 256
NT = S // P
EF = E // P
HEADS, DH, CHUNK = 16, 16, 64
NEXP, HID, CAP = 8, 1024, 2560
ROW = E + NEXP + 2
TOKENS = NB * S
TILE = 512
NTILE = CAP // TILE
KH = HID // P
EPS = 1e-5
BIG = 1e30
OOB = 1 << 20

NCH = S // CHUNK
PAIRS = 4
RING = 3


def win(y):
    return max(0, (y - 1) * CHUNK), min(S, (y + 2) * CHUNK)


def key_win(j):
    return max(0, 2 * j - 1), min(NCH, 2 * j + 3)


UNIT_CH = [(0, 1, 2, 3), (7, 4, 5, 6)]
UNIT_AT = []
for _chs in UNIT_CH:
    _at, _n = [], 0
    for _y in _chs:
        _at.append(_n)
        _n += win(_y)[1] - win(_y)[0]
    UNIT_AT.append(_at)
UNIT_W = _n
UNITS = [(2 * g + tt, hf) for g in range(2) for hf in range(2) for tt in range(2)]

_S = [[f"s{t}{j}" for j in range(NT)] for t in range(PAIRS)]
_COMMON = (["q", "k", "qs0", "ks0", "v", "ot_prev", "qs1", "ks1", "s00", "s01", "qs2", "ks2", "s02", "s03", "qs3", "ks3"]
           + _S[1])
ORDER = [_COMMON + _S[2] + ["px"] + _S[3] + ["mt", "ot", "xt0", "xt1"],
         _COMMON + ["x2t0"] + _S[2] + ["x2t1"] + _S[3] + ["lg", "mt", "ot"]]
assert (len(ORDER[0]) + len(ORDER[1])) % RING == 0


def bank_of(c, use):
    return (len(ORDER[0]) * c + ORDER[c].index(use)) % RING


def layer(nc, x, wqT, wkT, wvT, bqkv, wg, bg, w1, w2, w3, consts, out):
    c_ident, c_rep, c_kaux, c_qaux, c_tri, c_small = consts
    queue = nc.dram_tensor("queue", [NEXP * CAP, ROW], F32, kind="Internal").ap()
    x_v = x.rearrange("b (t p) e -> b p t e", p=P)
    out_v = out.rearrange("(n t p) e -> n p t e", t=NT, p=P)
    queue_v = queue.rearrange("(n t p) r -> n p t r", t=TILE // P, p=P)

    ctx = ExitStack()
    with ctx:
        def sb(name, shape, dt=F32, c=ctx):
            return c.enter_context(nc.sbuf_tensor(name, shape, dt))

        def sem(name):
            return ctx.enter_context(nc.semaphore(name))

        ident = sb("ident", [P, P])
        w_raw = sb("w_raw", [P, 3, 2048])
        zero_row = sb("zero_row", [P, NT, ROW])

        s_apart = sem("s_apart")

        def wait_apart(eng, of, value):
            eng.wait_ge(of, value)
            if type(value) is not int:
                eng.sem_inc(s_apart, 1)

        s_wraw = sem("s_wraw")

        w12_src = [w.rearrange("e (f p) h -> e p f h", p=P) for w in (w1, w2)]
        w3_src = w3.rearrange("e (k p) d -> e p k d", p=P)

        def load_expert(eng, e):
            e = slice(e, e + 1) if type(e) is int else e
            for n in range(2):
                eng.dma_start(w_raw[:, n, :].rearrange("p (f h) -> p f h", f=EF), w12_src[n][e, :, :, :])\
                   .then_inc(s_wraw, 16)
            eng.dma_start(w_raw[:, 2, :].rearrange("p (k d) -> p k d", k=KH), w3_src[e, :, :, :]).then_inc(s_wraw, 16)

        attention_phase(nc, w_raw, sem, ident, zero_row, x_v, wqT, wkT, wvT, bqkv, wg, bg,
                        c_ident, c_rep, c_kaux, c_qaux, c_tri, c_small, queue, queue_v, out, out_v,
                        load_expert, wait_apart)
        expert_phase(nc, sem, ident, w_raw, s_wraw, queue_v, out, load_expert, wait_apart)


def attention_phase(nc, w_raw, sem, ident, zero_row, x_v, wqT, wkT, wvT, bqkv, wg, bg,
                    c_ident, c_rep, c_kaux, c_qaux, c_tri, c_small, queue, queue_v, out, out_v,
                    load_expert, wait_apart):
    ctx = ExitStack()
    with ctx:
        def sb(name, shape, dt=F32):
            return ctx.enter_context(nc.sbuf_tensor(name, shape, dt))

        def pb(name, shape):
            return ctx.enter_context(nc.psum_tensor(name, shape, F32))

        w_q = w_raw[:, 0, 0:3 * EF * E].rearrange("p (n f o) -> p n f o", n=3, f=EF)
        b_raw = w_raw[0:1, 2, 0:3 * E].rearrange("p (n e) -> p n e", n=3)
        rep_f = w_raw[:, 1, 0:16 * 96].rearrange("p (n t m) -> p n t m", n=4, t=PAIRS)
        qaux_f = w_raw[:, 1, 16 * 96:16 * 96 + S]
        kaux_f = w_raw[:, 2, 3 * E:3 * E + 2 * S]
        w_qh = sb("w_qh", [P, 3, EF, E], F32R)
        w_ql = sb("w_ql", [P, 3, EF, E], F32R)
        b_lo = sb("b_lo", [1, 3, E], F32R)
        b_hl = sb("b_hl", [2, 3, E], F32R)
        ones2 = sb("ones2", [2, S], F32R)
        ones_f = sb("ones_f", [P, P])
        tri = sb("tri", [P, P])
        rep = sb("rep", [P, 4, PAIRS, 96], F32R)
        small = sb("small", [P, 90])
        c_floor = small[:, 0:32].rearrange("p (h j) -> p h j", h=8)
        c_cnt = small[:, 32:36]
        c_a, c_b = small[:, 36:37], small[:, 37:38]
        c_tok = small[:, 38:42]
        c_iota = small[:, 42:50]
        c_slot0 = small[:, 50:58]
        c_chunk = small[:, 58:74].rearrange("p (j c) -> p j c", j=NT)
        c_spare = small[:, 74:78]
        bg_t = sb("bg_t", [P, NEXP])
        wg_t = sb("wg_t", [P, EF, NEXP])

        xin = sb("xin", [P, NT, E])
        stats = sb("stats", [P, NT, 6])
        mv = sb("mv", [P, NT, 2])
        lnp = sb("lnp", [P, 3, NT])
        half_m = sb("half_m", [P, NT])
        xn = sb("xn", [P, NT, E])
        xth = sb("xth", [P, EF, S], F32R)
        xtl = sb("xtl", [P, EF, S], F32R)
        qbh, qbl, kbh, kbl = (sb(n, [P, S], F32R) for n in ("qbh", "qbl", "kbh", "kbl"))
        qst = [[sb(f"qst{c}{t}", [P, S], F32R) for t in range(PAIRS)] for c in range(2)]
        kst = [[sb(f"kst{c}{t}", [P, NCH, P], F32R) for t in range(PAIRS)] for c in range(2)]
        va = [sb(f"va{c}", [P, NCH, PAIRS, 64]) for c in range(2)]
        mraw = sb("mraw", [P, 8, NT])
        mx = sb("mx", [P, NT, P])
        negm = sb("negm", [P, 8, NT])
        epad = sb("epad", [P, 8, NT])
        pad = [sb(f"pad{c}", [P, 8, NT]) for c in range(2)]
        prob = [sb(f"prob{n}", [P, UNIT_W]) for n in range(4)]
        pv_sb = sb("pv_sb", [P, S])
        den = sb("den", [P, NT, 4])
        rden = sb("rden", [P, NT, 4])
        att = sb("att", [P, NT, E])
        xres = sb("xres", [P, NT, E])
        x1 = sb("x1", [P, NT, E])
        stats2 = sb("stats2", [P, NT, 6])
        mv2 = sb("mv2", [P, NT, 2])
        lnp2 = sb("lnp2", [P, 3, NT])
        x2n = sb("x2n", [P, NT, E])
        rows = sb("rows", [P, NT, ROW])
        x2t = sb("x2t", [P, EF, S])
        lg = sb("lg", [P, NT, NEXP])
        top = sb("top", [P, NT, 8])
        topi = sb("topi", [P, NT, 8], U32)
        topf = sb("topf", [P, NT, 2])
        hot = sb("hot", [P, 2, NT, NEXP])
        lab = sb("lab", [P, NT, NEXP])
        carry = sb("carry", [P, NT + 1, NEXP])
        dg = sb("dg", [P, NT])
        eg = sb("eg", [P, NT])
        gs = sb("gs", [P, NT])
        gw = sb("gw", [P, 2, NT])
        gt = sb("gt", [P, 2, NT, NEXP])
        px = sb("px", [P, NT, NEXP])
        ok = sb("ok", [P, NT, NEXP])
        slot = sb("slot", [P, NT, NEXP])
        slots = sb("slots", [P, 2, NT, NEXP])
        slotf = sb("slotf", [P, 2, NT])
        sloti = sb("sloti", [P, 2, NT], U32)
        tokf = sb("tokf", [P, NT])

        pst = [pb(f"pst{n}", [P, 1024]) for n in range(2)]
        pv = pb("pv", [P, 512])
        ring = [pb(f"ring{n}", [P, 512]) for n in range(RING)]

        s_const, s_cdve, s_blo, s_bhl, s_zero, s_fill, s_out0 = (
            sem(n) for n in ("s_const", "s_cdve", "s_blo", "s_bhl", "s_zero", "s_fill", "s_out0"))
        s_xin, s_xres = sem("s_xin"), sem("s_xres")
        s_st, s_mv = sem("s_st"), sem("s_mv")
        s_pg, s_xn = sem("s_pg"), sem("s_xn")
        s_xt, s_xth, s_xtl = sem("s_xt"), sem("s_xth"), sem("s_xtl")
        s_q, s_qh, s_ql = sem("s_q"), sem("s_qh"), sem("s_ql")
        s_k, s_kh, s_kl = sem("s_k"), sem("s_kh"), sem("s_kl")
        s_qs, s_qst = sem("s_qs"), sem("s_qst")
        s_ks, s_kst = sem("s_ks"), sem("s_kst")
        s_v, s_vc = sem("s_v"), sem("s_vc")
        s_s, s_mr = sem("s_s"), sem("s_mr")
        s_mx, s_mt, s_mta, s_mtd = sem("s_mx"), sem("s_mt"), sem("s_mta"), sem("s_mtd")
        s_neg, s_ep, s_pad = sem("s_neg"), sem("s_ep"), sem("s_pad")
        s_sc, s_ex = sem("s_sc"), sem("s_ex")
        s_pv, s_pvc = sem("s_pv"), sem("s_pvc")
        s_ot, s_at = sem("s_ot"), sem("s_at")
        s_dn = sem("s_dn")
        s_x1 = sem("s_x1")
        s_x1o = sem("s_x1o")
        s_x2r = sem("s_x2r")
        s_st2, s_mv2, s_pg2, s_x2 = sem("s_st2"), sem("s_mv2"), sem("s_pg2"), sem("s_x2")
        s_x2t, s_x2c = sem("s_x2t"), sem("s_x2c")
        s_lg, s_g, s_eg = sem("s_lg"), sem("s_g"), sem("s_eg")
        s_px = sem("s_px")
        s_scat = sem("s_scat")

        NCONST = 12
        G_STEPS = 18

        block = ctx.enter_context(nc.Block())

        @block.sync
        def _(sp):
            for n, w in enumerate((wqT, wkT, wvT)):
                sp.dma_start(w_q[:, n, :, :], w.rearrange("(f p) o -> p f o", p=P)).then_inc(s_const, 16)
            sp.dma_start(xin[:, :, :], x_v[0, :, :, :]).then_inc(s_xin, 16)
            sp.dma_start(ident[:, :], c_ident).then_inc(s_const, 16)
            sp.dma_start(b_raw[:, :, :], bqkv.rearrange("(a n) e -> a n e", a=1)).then_inc(s_const, 16)
            sp.dma_start(small[:, :], c_small).then_inc(s_const, 16)
            sp.dma_start(rep_f, c_rep).then_inc(s_const, 16)
            sp.dma_start(qaux_f[96:P, :], c_qaux).then_inc(s_const, 16)
            sp.dma_start(kaux_f[96:P, :], c_kaux).then_inc(s_const, 16)
            sp.dma_start(tri[:, :], c_tri).then_inc(s_const, 16)
            sp.dma_start(wg_t[:, :, :], wg.rearrange("(f p) e -> p f e", p=P)).then_inc(s_const, 16)
            sp.dma_start(bg_t[:, :], bg.rearrange("(a e) -> a e", a=1).to_broadcast([P, NEXP])).then_inc(s_const, 16)
            sp.wait_ge(s_blo, 1)
            sp.dma_start(b_hl[1:2, :, :].bitcast(F32), b_lo[:, :, :].bitcast(F32)).then_inc(s_bhl, 16)
            sp.dma_start(xres[:, :, :], x_v[0, :, :, :]).then_inc(s_xres, 16)
            load_expert(sp, 0)

            def loads(b):
                sp.wait_ge(s_xn, b + 1)
                sp.dma_start(xin[:, :, :], x_v[bass.ds((b + 1) % NB, 1), :, :, :]).then_inc(s_xin, 16)

            def stores(b):
                sp.wait_ge(s_x1, b + 1)
                sp.dma_start(out_v[bass.ds(b, 1), :, :, :], x1[:, :, :]).then_inc(s_x1o, 16)
                sp.dma_start(xres[:, :, :], x_v[bass.ds((b + 1) % NB, 1), :, :, :]).then_inc(s_xres, 16)

            loads(0)
            with sp.Fori(1, NB) as b:
                loads(b)
                stores(b - 1)
            loads(NB)
            stores(NB - 1)
            sp.wait_ge(s_x1o, 16 * NB)
            sp.wait_ge(s_xin, 16 * (NB + 2))
            sp.wait_ge(s_xres, 16 * (NB + 1))

        @block.gpsimd
        def _(g):
            g.memset(half_m[:, :], -0.5).then_inc(s_pg, 1)

            def norm_params(b, own, n0, ready, mvt, par):
                wait_apart(g, ready, b + 1)
                g.tensor_scalar(par[:, 0, :], mvt[:, :, 1], EPS, None, ALU.add).then_inc(own, 1)
                g.tensor_scalar(par[:, 2, :], mvt[:, :, 0], -1.0, None, ALU.mult).then_inc(own, 1)
                wait_apart(g, own, b * 3 + n0 + 2)
                g.tensor_tensor(par[:, 1, :], par[:, 0, :], half_m[:, :], ALU.pow).then_inc(own, 1)
                wait_apart(g, own, b * 3 + n0 + 3)

            def norm1(b):
                norm_params(b, s_pg, 1, s_mv, mv, lnp)
                if n_ge(b, 1):
                    wait_apart(g, s_xt, b * 2)
                for t in range(NT):
                    last = g.tensor_scalar(xn[:, t, :], xin[:, t, :], lnp[:, 2, t:t + 1], lnp[:, 1, t:t + 1],
                                           ALU.add, ALU.mult)
                last.then_inc(s_xn, 1)

            def residual(b):
                wait_apart(g, s_at, b * 4 + 4)
                wait_apart(g, s_xres, b * 16 + 16)
                if n_ge(b, 1):
                    wait_apart(g, s_x1o, b * 16)
                g.tensor_tensor(x1[:, :, :], xres[:, :, :], att[:, :, :], ALU.add).then_inc(s_x1, 1)

            def norm2(b):
                norm_params(b, s_pg2, 0, s_mv2, mv2, lnp2)
                if n_ge(b, 1):
                    wait_apart(g, s_x2t, b * 2)
                for t in range(NT):
                    last = g.tensor_scalar(x2n[:, t, :], x1[:, t, :], lnp2[:, 2, t:t + 1], lnp2[:, 1, t:t + 1],
                                           ALU.add, ALU.mult)
                last.then_inc(s_x2, 1)
                wait_apart(g, s_x2, b + 1)
                if n_ge(b, 1):
                    wait_apart(g, s_scat, b * (16 * 2 * NT))
                g.tensor_copy(rows[:, :, 0:E], x2n[:, :, :]).then_inc(s_x2r, 1)

            def dispatch(b):
                wait_apart(g, s_g, b * G_STEPS + G_STEPS)
                for k in range(2):
                    for t in range(NT):
                        g.indirect_dma_start(queue[:, :], bass.IndirectOffsetOnAxis(ap=sloti[:, k, t:t + 1], axis=0),
                                             rows[:, t, :], None, bounds_check=NEXP * CAP - 1, oob_is_err=False)\
                         .then_inc(s_scat, 16)

            norm1(0)
            norm1(1)
            wait_apart(g, s_fill, 16 * NEXP * NTILE)

            def turn(b):
                residual(b - 1)
                norm1(b + 1)
                if n_ge(b, 2):
                    dispatch(b - 2)
                norm2(b - 1)

            turn(1)
            with g.Fori(2, NB) as b:
                turn(b)
            residual(NB - 1)
            dispatch(NB - 2)
            norm2(NB - 1)
            dispatch(NB - 1)
            wait_apart(g, s_scat, 16 * 2 * NT * NB)
            wait_apart(g, s_out0, 16)

        @block.scalar
        def _(a):
            a.wait_ge(s_zero, 1)
            for n in range(NEXP * NTILE):
                a.dma_start(queue_v[n, :, :, :], zero_row[:, :, :]).then_inc(s_fill, 16)
            a.dma_start(out_v[NB, :, :, :], zero_row[:, :, 0:E]).then_inc(s_out0, 16)

            def high_part(n, c, use, full, done, dst, read):
                a.wait_ge(full, n + 1)
                if n_ge(n, 1):
                    a.wait_ge(read, 4 * n)
                a.activation(dst[:, :], ring[bank_of(1 - c, use)][:, :], ACT.Copy).then_inc(done, 1)

            def stacks(n, c, t):
                o = 1 - c
                a.wait_ge(s_qs, 4 * n + t + 1)
                if n_ge(n, 2):
                    a.wait_ge(s_sc, 8 * (n - 1))
                a.activation(qst[c][t][0:96, :], ring[bank_of(o, f"qs{t}")][0:96, :], ACT.Copy).then_inc(s_qst, 1)
                a.wait_ge(s_ks, 4 * n + t + 1)
                for h, of_head in enumerate((c_a, c_b)):
                    last = a.activation(kst[c][t][0:96, :, h * CHUNK:(h + 1) * CHUNK],
                                        ring[bank_of(o, f"ks{t}")][0:96, :].rearrange("p (y k) -> p y k", y=NCH),
                                        ACT.Copy, scale=of_head[0:96, :])
                last.then_inc(s_kst, 1)

            def v_part(n, c):
                a.wait_ge(s_v, n + 1)
                if n_ge(n, 2):
                    a.wait_ge(s_pv, 4 * (n - 1))
                src = ring[bank_of(1 - c, "v")][:, :].rearrange("p (j t h d) -> p j t h d", j=NT, t=PAIRS, h=2)
                for y2 in range(2):
                    for h in range(2):
                        dst = va[c][64 * h:64 * h + 64, y2:NCH:2, :, 32 * h:32 * h + DH]
                        last = a.activation(dst, src[64 * y2:64 * y2 + 64, :, :, h, :], ACT.Copy)
                last.then_inc(s_vc, 1)

            def exp(s, u):
                a.wait_ge(s_sc, s * 8 + u + 1)
                if n_ge(s, 1) or u >= 4:
                    a.wait_ge(s_pv, s * 4 + (u - 4) // 2 + 1)
                a.activation(prob[u % 4][:, :], pst[u % 2][:, 0:UNIT_W], ACT.Exp).then_inc(s_ex, 1)

            def pv_copy(g_):
                a.wait_ge(s_pv, g_ * 2 + 2)
                if n_ge(g_, 1):
                    a.wait_ge(s_ot, g_ * 1)
                a.activation(pv_sb[:, :], pv[:, :], ACT.Copy).then_inc(s_pvc, 1)

            def mt_copy(n, c):
                a.wait_ge(s_mt, n + 1)
                src = ring[bank_of(1 - c, "mt")]
                for t in (0, 1):
                    last = a.activation(qst[c][t][96:P, :], src[32 * t:32 * t + 32, :], ACT.Copy)
                last.then_inc(s_mta, 1)
                a.wait_ge(s_neg, n + 1)
                if n_ge(n, 1):
                    a.wait_ge(s_pad, n)
                a.activation(epad[:, :, :], negm[:, :, :], ACT.Exp).then_inc(s_ep, 1)

            def xt_part(b, f):
                a.wait_ge(s_xt, b * 2 + f + 1)
                if n_ge(b, 1):
                    a.wait_ge(s_v, b * 2)
                a.activation(xth[:, f, :], ring[bank_of(0, f"xt{f}")][:, :], ACT.Copy).then_inc(s_xth, 1)

            def x2_copy(b, f):
                a.wait_ge(s_x2t, b * 2 + f + 1)
                if n_ge(b, 1):
                    a.wait_ge(s_lg, b)
                a.activation(x2t[:, f, :], ring[bank_of(1, f"x2t{f}")][:, :], ACT.Copy).then_inc(s_x2c, 1)

            def gate_exp(b):
                a.wait_ge(s_g, b * G_STEPS + 3)
                a.activation(eg[:, :], dg[:, :], ACT.Exp).then_inc(s_eg, 1)

            def step(b, c, back, gating):
                s, nx, nc_ = b * 2 + c, b * 2 + c + 1, 1 - c
                exp(s, 0)
                if back or c:
                    pv_copy(2 * s - 1)
                high_parts(nx, nc_)
                exp(s, 1)
                stacks(nx, nc_, 0)
                v_part(nx, nc_)
                exp(s, 2)
                stacks(nx, nc_, 1)
                exp(s, 3)
                stacks(nx, nc_, 2)
                exp(s, 4)
                stacks(nx, nc_, 3)
                exp(s, 5)
                pv_copy(2 * s)
                if c and back:
                    x2_copy(b - 1, 0)
                if gating and c == 0:
                    gate_exp(b - 2)
                exp(s, 6)
                if c and back:
                    x2_copy(b - 1, 1)
                exp(s, 7)
                mt_copy(nx, nc_)
                if c == 0:
                    xt_part(b + 1, 0)
                    xt_part(b + 1, 1)

            def high_parts(n, c):
                high_part(n, c, "q", s_q, s_qh, qbh, s_qs)
                high_part(n, c, "k", s_k, s_kh, kbh, s_ks)

            xt_part(0, 0)
            xt_part(0, 1)
            high_parts(0, 0)
            stacks(0, 0, 0)
            v_part(0, 0)
            for t in range(1, PAIRS):
                stacks(0, 0, t)
            mt_copy(0, 0)
            step(0, 0, False, False)
            step(0, 1, False, False)
            step(1, 0, True, False)
            step(1, 1, True, False)
            with a.Fori(2, NB) as b:
                step(b, 0, True, True)
                step(b, 1, True, True)
            pv_copy(4 * NB - 1)
            gate_exp(NB - 2)
            x2_copy(NB - 1, 0)
            x2_copy(NB - 1, 1)
            gate_exp(NB - 1)
            a.wait_ge(s_fill, 16 * NEXP * NTILE)

        @block.vector
        def _(v):
            v.memset(zero_row[:, :, :], 0.0).then_inc(s_cdve, 1)
            v.memset(ones_f[:, :], 1.0)
            v.memset(carry[:, 0, :], 0.0)
            for c in range(2):
                v.memset(va[c][:, :, :, :], 0.0)
                for t in range(PAIRS):
                    v.memset(kst[c][t][:, :, :].bitcast(F32), 0.0)
                    v.memset(qst[c][t][:, :].bitcast(F32), 0.0)
            v.memset(rows[:, :, :], 0.0)
            v.memset(mx[:, :, :], 0.0).then_inc(s_cdve, 1)
            v.wait_ge(s_cdve, 2)
            for c in range(2):
                for h in range(2):
                    v.memset(va[c][64 * h:64 * h + 64, :, :, 32 * h + DH:32 * h + DH + 1], 1.0)
            v.wait_ge(s_const, 16 * NCONST)
            v.tensor_copy(ones2[:, :], ones_f[0:2, 0:1].to_broadcast([2, S]))
            v.tensor_scalar(w_q[:, 0, :, :], w_q[:, 0, :, :], DH ** -0.5, None, ALU.mult)
            v.tensor_scalar(b_raw[:, 0, :], b_raw[:, 0, :], DH ** -0.5, None, ALU.mult).then_inc(s_cdve, 1)
            v.wait_ge(s_cdve, 3)
            v.tensor_copy(w_qh[:, :, :, :], w_q[:, :, :, :])
            v.tensor_copy(b_hl[0:1, :, :], b_raw[:, :, :])
            v.tensor_copy(rep[:, :, :, :], rep_f)
            for c in range(2):
                for t in range(PAIRS):
                    v.tensor_copy(qst[c][t][96:P, :], qaux_f[96:P, :])
                    v.tensor_copy(kst[c][t][96:P, :, :], kaux_f[96:P, :].rearrange("p (y k) -> p y k", y=NCH))
            v.tensor_copy(tokf[:, :], c_tok)
            v.tensor_copy(zero_row[:, :, E + NEXP:E + NEXP + 1].bitcast(U32),
                          c_spare.unsqueeze(2)).then_inc(s_zero, 1)
            v.tensor_copy(mx[:, :, :].rearrange("p j (t r) -> p j t r", r=32)[:, :, :, 0:4],
                          c_chunk.unsqueeze(2).to_broadcast([P, NT, 4, 4])).then_inc(s_cdve, 1)
            v.wait_ge(s_cdve, 4)
            v.tensor_tensor(w_ql[:, :, :, :], w_q[:, :, :, :], w_qh[:, :, :, :].bitcast(F32), ALU.subtract)
            v.tensor_tensor(b_lo[:, :, :], b_raw[:, :, :], b_hl[0:1, :, :].bitcast(F32), ALU.subtract)\
             .then_inc(s_blo, 1)

            def stats_of(b, ready, dst, src, st, mvt, own_st, own_mv):
                v.wait_ge(ready[0], b * ready[1] + ready[1])
                for t in range(NT):
                    last = v.bn_stats(st[:, t, :], src[:, t, :])
                last.then_inc(own_st, 1)
                wait_apart(v, own_st, b + 1)
                for t in range(NT):
                    last = v.bn_aggr(mvt[:, t, :], st[:, t, :])
                last.then_inc(own_mv, 1)

            def norm1(b):
                if n_ge(b, 1):
                    v.wait_ge(s_xn, b)
                stats_of(b, (s_xin, 16), mv, xin, stats, mv, s_st, s_mv)

            def norm2(b):
                if n_ge(b, 1):
                    v.wait_ge(s_x2, b)
                stats_of(b, (s_x1, 1), mv2, x1, stats2, mv2, s_st2, s_mv2)

            def xt_part(b, f):
                v.wait_ge(s_xth, b * 2 + f + 1)
                v.tensor_tensor(xtl[:, f, :], ring[bank_of(0, f"xt{f}")][:, :], xth[:, f, :].bitcast(F32), ALU.subtract).then_inc(s_xtl, 1)

            def low_parts(n, c):
                for use, ready, done, hi, lo in (("q", s_qh, s_ql, qbh, qbl), ("k", s_kh, s_kl, kbh, kbl)):
                    v.wait_ge(ready, n + 1)
                    v.tensor_tensor(lo[:, :], ring[bank_of(1 - c, use)][:, :], hi[:, :].bitcast(F32),
                                    ALU.subtract).then_inc(done, 1)

            def maxima(n, c, t, js):
                for j in js:
                    y0, y1 = key_win(j)
                    v.wait_ge(s_s, n * 16 + t * 4 + j + 1)
                    if t == 0 and j == 0 and n_ge(n, 1):
                        v.wait_ge(s_mx, n)
                    v.tensor_reduce(mraw[:, 2 * t:2 * t + 2, j],
                                    ring[bank_of(1 - c, f"s{t}{j}")][:, 0:(y1 - y0) * P]
                                    .rearrange("p (y h k) -> p h y k", h=2, k=CHUNK), AX.XY, ALU.max).then_inc(s_mr, 1)

            def mx_of(n, c):
                v.wait_ge(s_mr, n * 16 + 16)
                if n_ge(n, 1):
                    v.wait_ge(s_mt, n)
                mxm = mx[:, :, :].rearrange("p j (t r) -> p t r j", r=32)[:, :, 4:6, :]
                v.tensor_tensor(mxm.bitcast(F32R), mraw[:, :, :].rearrange("p (t h) j -> p t h j", h=2),
                                c_floor.rearrange("p (t h) j -> p t h j", h=2), ALU.max).then_inc(s_mx, 1)
                v.wait_ge(s_mx, n + 1)
                if n_ge(n, 1):
                    v.wait_ge(s_ep, n)
                v.tensor_scalar(negm[:, :, :].rearrange("p (t h) j -> p t h j", h=2), mxm,
                                -1.0, 0.0, ALU.mult, ALU.min).then_inc(s_neg, 1)

            def mt_copy(n, c):
                v.wait_ge(s_mta, n + 1)
                src = ring[bank_of(1 - c, "mt")]
                for t in (2, 3):
                    last = v.tensor_copy(qst[c][t][96:P, :], src[32 * t:32 * t + 32, :])
                last.then_inc(s_mtd, 1)

            def pad_of(n, c):
                v.wait_ge(s_ep, n + 1)
                v.tensor_tensor(pad[c][:, :, :], epad[:, :, :],
                                c_cnt.unsqueeze(1).to_broadcast([P, 8, NT]), ALU.mult).then_inc(s_pad, 1)

            def quotient(g_, c, grp, b, step_, pm):
                o = pm[:, :].rearrange("p (j h d) -> p j h d", j=NT, d=32)
                h0 = 4 * grp
                v.wait_ge(s_ot, g_ + 1)
                v.wait_ge(s_pad, step_ + 1)
                v.tensor_tensor(den[:, :, :], o[:, :, :, DH], pad[c][:, h0:h0 + 4, :].rearrange("p h j -> p j h"),
                                ALU.add).then_inc(s_dn, 1)
                v.wait_ge(s_dn, g_ * 2 + 1)
                v.reciprocal(rden[:, :, :], den[:, :, :]).then_inc(s_dn, 1)
                v.wait_ge(s_dn, g_ * 2 + 2)
                if c == 0 and grp == 0 and n_ge(b, 1):
                    v.wait_ge(s_x1, b)
                at = c * P + h0 * DH
                v.tensor_tensor(att[:, :, at:at + 4 * DH].rearrange("p j (h d) -> p j h d", h=4),
                                o[:, :, :, 0:DH], rden[:, :, :].unsqueeze(3).to_broadcast([P, NT, 4, DH]),
                                ALU.mult).then_inc(s_at, 1)

            def gate_step(b, n):
                per_expert = [P, NT, NEXP]
                if n > 1:
                    wait_apart(v, s_g, b * G_STEPS + n - 1)
                if n == 1:
                    v.wait_ge(s_lg, b + 1)
                    last = v.tensor_tensor(lg[:, :, :],
                                           ring[bank_of(1, "lg")][:, 0:NT * NEXP].rearrange("p (t e) -> p t e", t=NT),
                                           bg_t[:, :].unsqueeze(1).to_broadcast(per_expert), ALU.add)
                elif n == 2:
                    for t in range(NT):
                        last = v.max(top[:, t, :], lg[:, t, :])
                elif n == 3:
                    last = v.tensor_tensor(dg[:, :], top[:, :, 1], top[:, :, 0], ALU.subtract)
                elif n == 4:
                    for t in range(NT):
                        last = v.max_index(topi[:, t, :], top[:, t, :], lg[:, t, :])
                elif n == 5:
                    last = v.tensor_copy(topf[:, :, :], topi[:, :, 0:2])
                elif n == 6:
                    for kk in range(2):
                        last = v.tensor_tensor(hot[:, kk, :, :], c_iota.unsqueeze(1).to_broadcast(per_expert),
                                               topf[:, :, kk:kk + 1].to_broadcast(per_expert), ALU.is_equal)
                elif n == 7:
                    if n_ge(b, 1):
                        v.wait_ge(s_px, b)
                    last = v.tensor_tensor(lab[:, :, :], hot[:, 0, :, :], hot[:, 1, :, :], ALU.add)
                elif n < 12:
                    t = n - 8
                    last = v.tensor_tensor(carry[:, t + 1, :], carry[:, t, :], lab[:, t, :], ALU.add)
                elif n == 12:
                    v.wait_ge(s_px, b + 1)
                    p3 = ring[bank_of(0, "px")][:, 0:NT * NEXP].rearrange("p (t e) -> p t e", t=NT)
                    v.tensor_copy(carry[:, 0, :], carry[:, NT, :])
                    v.tensor_scalar(ok[:, :, :], p3, float(CAP), float(OOB), ALU.is_gt, ALU.mult)
                    last = v.tensor_tensor(px[:, :, :], p3, c_slot0.unsqueeze(1).to_broadcast(per_expert), ALU.add)
                elif n == 13:
                    v.wait_ge(s_eg, b + 1)
                    v.tensor_scalar(gs[:, :], eg[:, :], 1.0, None, ALU.add)
                    last = v.tensor_tensor(slot[:, :, :], px[:, :, :], ok[:, :, :], ALU.add)
                elif n == 14:
                    v.reciprocal(gw[:, 0, :], gs[:, :])
                    last = v.tensor_tensor(slots[:, :, :, :].rearrange("p k t e -> p k (t e)"),
                                           hot[:, :, :, :].rearrange("p k t e -> p k (t e)"),
                                           slot[:, :, :].rearrange("p t e -> p (t e)").unsqueeze(1)
                                           .to_broadcast([P, 2, NT * NEXP]), ALU.mult)
                elif n == 15:
                    v.tensor_tensor(gw[:, 1, :], gw[:, 0, :], eg[:, :], ALU.mult)
                    last = v.tensor_reduce(slotf[:, :, :], slots[:, :, :, :], AX.X, ALU.add)
                elif n == 16:
                    for kk in range(2):
                        last = v.tensor_tensor(gt[:, kk, :, :], hot[:, kk, :, :],
                                               gw[:, kk, :].unsqueeze(2).to_broadcast(per_expert), ALU.mult)
                elif n == 17:
                    v.wait_ge(s_x2r, b + 1)
                    v.tensor_copy(sloti[:, :, :], slotf[:, :, :])
                    v.tensor_tensor(rows[:, :, E:E + NEXP], gt[:, 0, :, :], gt[:, 1, :, :], ALU.add)
                    last = v.tensor_copy(rows[:, :, E + NEXP:E + NEXP + 1].bitcast(U32), tokf[:, :].unsqueeze(2))
                else:
                    last = v.tensor_scalar(tokf[:, :], tokf[:, :], float(S), None, ALU.add)
                last.then_inc(s_g, 1)

            def step(b, c, back, gating):
                s, nx, nc_ = b * 2 + c, b * 2 + c + 1, 1 - c
                gating = gating and c == 0
                pad_of(s, c)
                low_parts(nx, nc_)
                if back or c:
                    quotient(2 * s - 1, 1 - c, 1, b if c else b - 1, s - 1, ring[bank_of(c, "ot_prev")])
                for t in range(PAIRS):
                    if t == 2 and c == 1:
                        norm1(b + 2)
                    if t == 3 and c == 0 and back:
                        norm2(b - 1)
                    for j in range(NT):
                        maxima(nx, nc_, t, (j,))
                        n = t * NT + j
                        if gating and (n < 10 or n >= 11):
                            gate_step(b - 2, n + 2 if n < 10 else n + 1)
                mx_of(nx, nc_)
                mt_copy(nx, nc_)
                if c and back:
                    gate_step(b - 1, 1)
                quotient(2 * s, c, 0, b, s, ring[bank_of(c, "ot")])
                if gating:
                    gate_step(b - 2, 17)
                    gate_step(b - 2, 18)
                if c == 0:
                    xt_part(b + 1, 0)
                    xt_part(b + 1, 1)

            norm1(0)
            xt_part(0, 0)
            xt_part(0, 1)
            low_parts(0, 0)
            for t in range(PAIRS):
                maxima(0, 0, t, range(NT))
            mx_of(0, 0)
            mt_copy(0, 0)
            norm1(1)
            step(0, 0, False, False)
            step(0, 1, False, False)
            step(1, 0, True, False)
            step(1, 1, True, False)
            with v.Fori(2, NB) as b:
                step(b, 0, True, True)
                step(b, 1, True, True)
            pad_of(2 * NB, 0)
            quotient(4 * NB - 1, 1, 1, NB - 1, 2 * NB - 1, ring[bank_of(0, "ot_prev")])
            for n in range(2, G_STEPS + 1):
                gate_step(NB - 2, n)
            norm2(NB - 1)
            for n in range(1, G_STEPS + 1):
                gate_step(NB - 1, n)

        @block.tensor
        def _(pe):
            last_use = [None] * RING
            passed = [0]

            def use(c, name, reader):
                n = bank_of(c, name)
                if last_use[n] is not None:
                    (of, value, per_seq), at = last_use[n]
                    pe.wait_ge(of, value if at is passed[0] else passed[0] * per_seq + value)
                last_use[n] = (reader, passed[0])
                return ring[n]

            def transposes(b, f, c, name, src, full, ready, free):
                pe.wait_ge(ready, b + 1)
                dst = use(c, name, (free, b * 2 + f + 1, 2))
                for t in range(NT):
                    last = pe.transpose(dst[:, t * P:(t + 1) * P], src[:, t, f * P:(f + 1) * P], ident[:, :])
                last.then_inc(full, 1)

            def qk(n, c, which, name, full, free):
                dst = use(1 - c, name, (free, n + 1, 2))
                if c == 0 and which == 0:
                    pe.wait_ge(s_xtl, n + 2)
                for f in range(EF):
                    for i, (w, xx) in enumerate(((w_qh, xth), (w_ql, xth), (w_qh, xtl))):
                        pe.matmul(dst[:, :], w[:, which, f, c * P:(c + 1) * P], xx[:, f, :],
                                  start=(f == 0 and i == 0), stop=False)
                pe.matmul(dst[:, :], b_hl[0:2, which, c * P:(c + 1) * P], ones2[0:2, :],
                          start=False, stop=True).then_inc(full, 1)

            def vv(n, c):
                dst = use(1 - c, "v", (s_vc, n + 1, 2))
                for t in range(NT):
                    ts = slice(t * P, (t + 1) * P)
                    for f in range(EF):
                        for i, (w, xx) in enumerate(((w_qh, xth), (w_ql, xth), (w_qh, xtl))):
                            pe.matmul(dst[:, ts], xx[:, f, ts], w[:, 2, f, c * P:(c + 1) * P],
                                      start=(f == 0 and i == 0), stop=False)
                    last = pe.matmul(dst[:, ts], ones2[0:2, 0:P], b_hl[0:2, 2, c * P:(c + 1) * P],
                                     start=False, stop=True)
                last.then_inc(s_v, 1)

            def stacks(n, c, t):
                if t == 0:
                    pe.wait_ge(s_ql, n + 1)
                dst = use(1 - c, f"qs{t}", (s_qst, 4 * n + t + 1, 8))
                pe.matmul(dst[0:96, :], rep[:, 0, t, :], qbh[:, :], start=True, stop=False)
                pe.matmul(dst[0:96, :], rep[:, 1, t, :], qbl[:, :], start=False, stop=True).then_inc(s_qs, 1)
                if t == 0:
                    pe.wait_ge(s_kl, n + 1)
                dst = use(1 - c, f"ks{t}", (s_kst, 4 * n + t + 1, 8))
                pe.matmul(dst[0:96, :], rep[:, 2, t, :], kbh[:, :], start=True, stop=False)
                pe.matmul(dst[0:96, :], rep[:, 3, t, :], kbl[:, :], start=False, stop=True).then_inc(s_ks, 1)

            def score_max(n, c, t, js):
                for j in js:
                    if j == js[0]:
                        pe.wait_ge(s_qst, 4 * n + t + 1)
                        wait_apart(pe, s_kst, 4 * n + t + 1)
                    y0, y1 = key_win(j)
                    dst = use(1 - c, f"s{t}{j}", (s_mr, 16 * n + 4 * t + j + 1, 32))
                    pe.matmul(dst[:, 0:(y1 - y0) * P], qst[c][t][0:100, j * P:(j + 1) * P],
                              kst[c][t][0:100, y0:y1, :].rearrange("p y k -> p (y k)"),
                              start=True, stop=True).then_inc(s_s, 1)

            def score(s, c, u):
                t, hf = UNITS[u]
                if u == 0:
                    pe.wait_ge(s_mta, s + 1)
                if u == 4:
                    pe.wait_ge(s_mtd, s + 1)
                if n_ge(s, 1) or u >= 2:
                    pe.wait_ge(s_ex, s * 8 + u - 1)
                for y, at in zip(UNIT_CH[hf], UNIT_AT[hf]):
                    lo, hi = win(y)
                    last = pe.matmul(pst[u % 2][:, at:at + hi - lo], kst[c][t][:, y, :], qst[c][t][:, lo:hi],
                                     start=True, stop=True)
                last.then_inc(s_sc, 1)

            def prob_v(s, c, n):
                g, hf = n // 2, n % 2
                if n == 0:
                    pe.wait_ge(s_vc, s + 1)
                if hf == 0 and (n_ge(s, 1) or g):
                    pe.wait_ge(s_pvc, s * 2 + g)
                pe.wait_ge(s_ex, s * 8 + 2 * n + 2)
                for i, (y, at) in enumerate(zip(UNIT_CH[hf], UNIT_AT[hf])):
                    lo, hi = win(y)
                    for tt in range(2):
                        last = pe.matmul(pv[64 * tt:64 * tt + 64, lo:hi], va[c][:, y, 2 * g + tt, :],
                                         prob[(2 * n + tt) % 4][:, at:at + hi - lo],
                                         start=(hf == 0 and i == 0), stop=(hf == 1 and i == 3),
                                         skip_group_check=True)
                last.then_inc(s_pv, 1)

            def out_t(g_, c, name):
                pe.wait_ge(s_pvc, g_ + 1)
                dst = use(c, name, (s_at, g_ + 1, 4))
                for j in range(NT):
                    last = pe.transpose(dst[:, j * P:(j + 1) * P], pv_sb[:, j * P:(j + 1) * P], ident[:, :])
                last.then_inc(s_ot, 1)

            def max_t(n, c):
                pe.wait_ge(s_mx, n + 1)
                dst = use(1 - c, "mt", (s_mtd, n + 1, 2))
                for j in range(NT):
                    last = pe.transpose(dst[:, j * P:(j + 1) * P], mx[:, j, :], ident[:, :])
                last.then_inc(s_mt, 1)

            def logits(b):
                pe.wait_ge(s_x2c, b * 2 + 2)
                dst = use(1, "lg", (s_g, b * G_STEPS + 1, G_STEPS))
                for t in range(NT):
                    for f in range(EF):
                        last = pe.matmul(dst[:, t * NEXP:(t + 1) * NEXP], x2t[:, f, t * P:(t + 1) * P],
                                         wg_t[:, f, :], start=(f == 0), stop=(f == EF - 1))
                last.then_inc(s_lg, 1)

            def counts(b):
                pe.wait_ge(s_g, b * G_STEPS + 11)
                dst = use(0, "px", (s_g, b * G_STEPS + 12, G_STEPS))
                pe.matmul(dst[:, 0:NT * NEXP], tri[:, :], lab[:, :, :].rearrange("p t e -> p (t e)"),
                          start=True, stop=False)
                pe.matmul(dst[:, 0:NT * NEXP], ones_f[:, :], carry[:, 0:NT, :].rearrange("p t e -> p (t e)"),
                          start=False, stop=True).then_inc(s_px, 1)

            def x_t(b, f):
                transposes(b, f, 0, f"xt{f}", xn, s_xt, s_xn, s_xtl)

            def x2_t(b, f):
                transposes(b, f, 1, f"x2t{f}", x2n, s_x2t, s_x2, s_x2c)

            def step(b, c, back, gating):
                s, nx, nc_ = b * 2 + c, b * 2 + c + 1, 1 - c
                score(s, c, 0)
                if back or c:
                    prob_v(s - 1, 1 - c, 3)
                qk(nx, nc_, 0, "q", s_q, s_ql)
                qk(nx, nc_, 1, "k", s_k, s_kl)
                score(s, c, 1)
                stacks(nx, nc_, 0)
                vv(nx, nc_)
                score(s, c, 2)
                if back or c:
                    out_t(2 * s - 1, c, "ot_prev")
                stacks(nx, nc_, 1)
                score_max(nx, nc_, 0, (0, 1))
                score(s, c, 3)
                stacks(nx, nc_, 2)
                prob_v(s, c, 0)
                score_max(nx, nc_, 0, (2, 3))
                score(s, c, 4)
                stacks(nx, nc_, 3)
                score_max(nx, nc_, 1, (0, 1))
                score(s, c, 5)
                score_max(nx, nc_, 1, (2, 3))
                if c and back:
                    x2_t(b - 1, 0)
                prob_v(s, c, 1)
                score_max(nx, nc_, 2, (0, 1))
                score(s, c, 6)
                score_max(nx, nc_, 2, (2, 3))
                if c and back:
                    x2_t(b - 1, 1)
                if gating and c == 0:
                    counts(b - 2)
                score(s, c, 7)
                score_max(nx, nc_, 3, range(NT))
                prob_v(s, c, 2)
                if c and back:
                    logits(b - 1)
                max_t(nx, nc_)
                out_t(2 * s, c, "ot")
                if c == 0:
                    x_t(b + 1, 0)
                    x_t(b + 1, 1)

            pe.wait_ge(s_blo, 1)
            pe.wait_ge(s_bhl, 16)
            x_t(0, 0)
            x_t(0, 1)
            qk(0, 0, 0, "q", s_q, s_ql)
            qk(0, 0, 1, "k", s_k, s_kl)
            stacks(0, 0, 0)
            vv(0, 0)
            for t in range(1, PAIRS):
                stacks(0, 0, t)
            for t in range(PAIRS):
                score_max(0, 0, t, range(NT))
            max_t(0, 0)
            step(0, 0, False, False)
            step(0, 1, False, False)
            step(1, 0, True, False)
            step(1, 1, True, False)
            with pe.Fori(2, NB) as b:
                passed[0] = b - 2
                step(b, 0, True, True)
                step(b, 1, True, True)
            last_use[:] = [None] * RING
            for of, value in ((s_at, 4 * NB - 1), (s_xtl, 2 * NB + 2), (s_mtd, 2 * NB + 1),
                              (s_g, G_STEPS * (NB - 2) + 1)):
                pe.wait_ge(of, value)
            prob_v(2 * NB - 1, 1, 3)
            out_t(4 * NB - 1, 0, "ot_prev")
            counts(NB - 2)
            x2_t(NB - 1, 0)
            x2_t(NB - 1, 1)
            logits(NB - 1)
            counts(NB - 1)


def n_ge(n, k):
    return type(n) is not int or n >= k


def expert_phase(nc, sem, ident, w_raw, s_wraw, queue_v, out, load_expert, wait_apart):
    ctx = ExitStack()
    with ctx:
        def sb(name, shape, dt=F32):
            return ctx.enter_context(nc.sbuf_tensor(name, shape, dt))

        def pb(name, shape):
            return ctx.enter_context(nc.psum_tensor(name, shape, F32))

        TT = TILE // P
        wh = [sb(f"wh{q}", [P, 3, 2048], F32R) for q in range(2)]
        wl = [sb(f"wl{q}", [P, 3, 2048], F32R) for q in range(2)]
        din = sb("din", [P, TT, ROW])
        tgate = sb("tgate", [P, TT, 1])
        ttok = sb("ttok", [P, TT, 1], U32)
        dxh = sb("dxh", [P, EF, TILE], F32R)
        dxl = sb("dxl", [P, EF, TILE], F32R)
        sg = [sb(f"sg{n}", [P, TILE]) for n in range(2)]
        gsg = [sb(f"gsg{n}", [P, TILE]) for n in range(2)]
        hf = [sb(f"hf{n}", [P, TILE]) for n in range(2)]
        HR = 4
        hh = [sb(f"hh{n}", [P, TILE], F32R) for n in range(HR)]
        hl = [sb(f"hl{n}", [P, TILE], F32R) for n in range(HR)]
        ys = sb("ys", [P, TT, E])

        pg = [pb(f"pg{n}", [P, TILE]) for n in range(2)]
        pu = [pb(f"pu{n}", [P, TILE]) for n in range(2)]
        px = pb("pxt", [P, EF, TILE])
        py = pb("py", [P, TT, E])

        s_wh = sem("s_wh")
        s_wsplit = sem("s_wsplit")
        s_din = sem("s_din")
        s_tail = sem("s_tail")
        s_dt = sem("s_dt")
        s_dh, s_dl = sem("s_dh"), sem("s_dl")
        s_up = sem("s_up")
        s_sg, s_gg, s_hf, s_hh, s_hl = (sem(n) for n in ("s_sg", "s_gg", "s_hf", "s_hh", "s_hl"))
        s_dn2 = sem("s_down")
        s_ys = sem("s_ys")
        s_add = sem("s_add")
        ALL = NEXP * NTILE

        block = ctx.enter_context(nc.Block())

        @block.sync
        def _(sp):
            sp.dma_start(din[:, :, :], queue_v[0, :, :, :]).then_inc(s_din, 16)
            with sp.Fori(0, NEXP) as e:
                sp.wait_ge(s_wsplit, e * 3 + 3)
                nxt = sp.snap((e + 1) % NEXP)
                load_expert(sp, bass.ds(nxt, 1))
                with sp.Fori(0, NTILE) as i:
                    n = e * NTILE + i
                    sp.wait_ge(s_tail, n + 1)
                    sp.wait_ge(s_dt, n * 2 + 2)
                    m = sp.snap((n + 1) % ALL)
                    sp.dma_start(din[:, :, :], queue_v[bass.ds(m, 1), :, :, :]).then_inc(s_din, 16)
            sp.wait_ge(s_din, 16 * (ALL + 1))
            sp.wait_ge(s_wraw, 48 * (NEXP + 1))

        @block.gpsimd
        def _(g):
            def split_expert(q, e):
                wait_apart(g, s_wraw, e * 48 + 48)
                for n in range(3):
                    g.tensor_copy(wh[q][:, n, :], w_raw[:, n, :]).then_inc(s_wh, 1)
                wait_apart(g, s_wh, e * 3 + 3)
                for n in range(3):
                    g.tensor_tensor(wl[q][:, n, :], w_raw[:, n, :], wh[q][:, n, :].bitcast(F32), ALU.subtract)\
                     .then_inc(s_wsplit, 1)

            def add_rows(n):
                wait_apart(g, s_ys, n + 1)
                if n_ge(n, 1):
                    wait_apart(g, s_add, n * (16 * TT))
                for t in range(TT):
                    g.indirect_dma_start(out[:, :], bass.IndirectOffsetOnAxis(ap=ttok[:, t, :], axis=0),
                                         ys[:, t, :], None, compute_op=ALU.add).then_inc(s_add, 16)

            def expert(e, q):
                if n_ge(e, 1):
                    wait_apart(g, s_dn2, e * (NTILE * KH))
                else:
                    g.wait_ge(s_wsplit, 3)
                split_expert(1 - q, e + 1)
                if type(e) is int and e == 0:
                    add_rows(0)
                with g.Fori(int(type(e) is int and e == 0), NTILE) as i:
                    add_rows(e * NTILE + i)

            expert(0, 0)
            expert(1, 1)
            with g.Fori(1, NEXP // 2) as ep:
                for q in range(2):
                    expert(ep * 2 + q, q)
            wait_apart(g, s_add, ALL * 16 * TT)

        @block.scalar
        def _(a):
            def x_part(n):
                for f in range(EF):
                    a.wait_ge(s_dt, n * 2 + f + 1)
                    a.activation(dxh[:, f, :], px[:, f, :], ACT.Copy).then_inc(s_dh, 1)

            def sigmoid(n, k):
                a.wait_ge(s_up, n * KH + k + 1)
                if n_ge(n, 1) or k >= 2:
                    a.wait_ge(s_gg, n * KH + k - 1)
                a.activation(sg[k % 2][:, :], pg[k % 2][:, :], ACT.Sigmoid).then_inc(s_sg, 1)

            def h_high(n, k):
                a.wait_ge(s_hf, n * KH + k + 1)
                if n_ge(n, 1) or k >= HR:
                    a.wait_ge(s_dn2, n * KH + k - HR + 1)
                a.activation(hh[k % HR][:, :], hf[k % 2][:, :], ACT.Copy).then_inc(s_hh, 1)

            def y_out(n):
                a.wait_ge(s_dn2, n * KH + KH)
                a.wait_ge(s_tail, n + 1)
                if n_ge(n, 1):
                    a.wait_ge(s_add, n * (16 * TT))
                for t in range(TT):
                    last = a.activation(ys[:, t, :], py[:, t, :], ACT.Copy, scale=tgate[:, t, :])
                last.then_inc(s_ys, 1)

            def tile(n):
                for k in range(KH):
                    sigmoid(n, k)
                    if k:
                        h_high(n, k - 1)
                h_high(n, KH - 1)
                x_part(n + 1)
                y_out(n)

            a.wait_ge(s_wraw, 48)
            for n in range(3):
                a.activation(wh[0][:, n, :], w_raw[:, n, :], ACT.Copy).then_inc(s_wh, 1)
            x_part(0)
            tile(0)
            with a.Fori(1, ALL) as n:
                tile(n)

        @block.vector
        def _(v):
            def x_part(n):
                for f in range(EF):
                    v.wait_ge(s_dh, n * 2 + f + 1)
                    v.tensor_tensor(dxl[:, f, :], px[:, f, :], dxh[:, f, :].bitcast(F32), ALU.subtract).then_inc(s_dl, 1)

            def silu_mul(n, k):
                v.wait_ge(s_sg, n * KH + k + 1)
                v.tensor_tensor(gsg[k % 2][:, :], pg[k % 2][:, :], sg[k % 2][:, :], ALU.mult).then_inc(s_gg, 1)
                v.wait_ge(s_gg, n * KH + k + 1)
                if n_ge(n, 1) or k >= 2:
                    v.wait_ge(s_hh, n * KH + k - 1)
                v.tensor_tensor(hf[k % 2][:, :], gsg[k % 2][:, :], pu[k % 2][:, :], ALU.mult).then_inc(s_hf, 1)

            def h_low(n, k):
                v.wait_ge(s_hh, n * KH + k + 1)
                v.tensor_tensor(hl[k % HR][:, :], hf[k % 2][:, :], hh[k % HR][:, :].bitcast(F32), ALU.subtract)\
                 .then_inc(s_hl, 1)

            def tail(n, e):
                v.wait_ge(s_din, n * 16 + 16)
                if n_ge(n, 1):
                    v.wait_ge(s_add, n * (16 * TT))
                v.tensor_copy(tgate[:, :, :], din[:, :, bass.ds(e + E, 1)])
                v.tensor_copy(ttok[:, :, :], din[:, :, E + NEXP:E + NEXP + 1].bitcast(U32)).then_inc(s_tail, 1)

            def tile(n, e):
                for k in range(KH):
                    silu_mul(n, k)
                    if k:
                        h_low(n, k - 1)
                    if k == 3:
                        tail(n, e)
                h_low(n, KH - 1)
                x_part(n + 1)

            for n in range(3):
                v.wait_ge(s_wh, n + 1)
                v.tensor_tensor(wl[0][:, n, :], w_raw[:, n, :], wh[0][:, n, :].bitcast(F32), ALU.subtract)\
                 .then_inc(s_wsplit, 1)
            x_part(0)
            tile(0, 0)
            with v.Fori(1, NTILE) as i:
                tile(i, 0)
            with v.Fori(1, NEXP) as e:
                ecol = v.snap(e + 0)
                with v.Fori(0, NTILE) as i:
                    tile(ecol * NTILE + i, ecol)

        @block.tensor
        def _(pe):
            def transposes(n):
                pe.wait_ge(s_din, n * 16 + 16)
                if n_ge(n, 1):
                    pe.wait_ge(s_dl, n * 2)
                for f in range(EF):
                    for t in range(TT):
                        last = pe.transpose(px[:, f, t * P:(t + 1) * P], din[:, t, f * P:(f + 1) * P], ident[:, :])
                    last.then_inc(s_dt, 1)

            def up(n, q, k):
                if k == 0:
                    pe.wait_ge(s_dl, n * 2 + 2)
                if n_ge(n, 1) or k >= 2:
                    pe.wait_ge(s_hf, n * KH + k - 1)
                for m, dst in enumerate((pg, pu)):
                    for f in range(EF):
                        cols = slice(f * HID + k * P, f * HID + (k + 1) * P)
                        for i, (w, xx) in enumerate(((wh, dxh), (wl, dxh), (wh, dxl))):
                            last = pe.matmul(dst[k % 2][:, :], w[q][:, m, cols], xx[:, f, :],
                                             start=(f == 0 and i == 0), stop=(f == EF - 1 and i == 2))
                last.then_inc(s_up, 1)

            def down(n, q, k):
                pe.wait_ge(s_hl, n * KH + k + 1)
                if k == 0 and n_ge(n, 1):
                    pe.wait_ge(s_ys, n)
                for i, (h, w) in enumerate(((hh, wh), (hh, wl), (hl, wh))):
                    for t in range(TT):
                        last = pe.matmul(py[:, t, :], h[k % HR][:, t * P:(t + 1) * P], w[q][:, 2, k * E:(k + 1) * E],
                                         start=(k == 0 and i == 0 and t % 2 == 0), stop=(k == KH - 1 and i == 2),
                                         skip_group_check=True)
                last.then_inc(s_dn2, 1)

            def tile(n, q):
                for k in range(KH):
                    up(n, q, k)
                    if k >= 2:
                        down(n, q, k - 2)
                transposes(n + 1)
                down(n, q, KH - 2)
                down(n, q, KH - 1)

            transposes(0)
            pe.wait_ge(s_wsplit, 3)
            tile(0, 0)
            with pe.Fori(1, NTILE) as i:
                tile(i, 0)
            pe.wait_ge(s_wsplit, 6)
            with pe.Fori(NTILE, 2 * NTILE) as i:
                tile(i, 1)
            with pe.Fori(1, NEXP // 2) as ep:
                for q in range(2):
                    e = ep * 2 + q
                    wait_apart(pe, s_wsplit, e * 3 + 3)
                    with pe.Fori(0, NTILE) as i:
                        tile(e * NTILE + i, q)


def kernel(**inputs):
    import numpy as np
    import concourse.bacc as bacc
    from concourse.bass_utils import run_bass_kernel_spmd as run

    a = {k: np.ascontiguousarray(v) for k, v in inputs.items()}
    p = np.arange(P)
    f32 = np.float32
    half = p // CHUNK
    rep = np.zeros((P, 4, PAIRS, 96), f32)
    d = np.arange(DH)
    for which, kinds in enumerate(((0, 1), (2,), (0, 2), (1,))):
        for t in range(PAIRS):
            for h in range(2):
                for kind in kinds:
                    rep[(2 * t + h) * DH + d, which, t, 48 * h + DH * kind + d] = 1.0
    m4 = np.arange(4)
    kaux = np.zeros((32, NCH, 2, CHUNK), f32)
    kaux[:4] = (np.arange(NCH)[None, :] % 4 == m4[:, None])[:, :, None, None]
    kaux[4, :, 0], kaux[5, :, 1] = -1.0, -1.0
    hidden = (np.arange(NCH)[:, None] % 4 == (m4[None, :] + 2) % 4)
    qaux = np.zeros((32, S), f32)
    qaux[:4] = np.where(np.repeat(hidden, CHUNK, axis=0).T, -BIG, 0.0)
    q_mask = np.where(hidden[2 * np.arange(NT)[None, :] + half[:, None]], -BIG, 0.0).astype(f32)
    cnt = np.zeros((P, NT), f32)
    cnt[:CHUNK, 0] = p[:CHUNK]
    cnt[CHUNK:, NT - 1] = CHUNK - 1 - p[:CHUNK]
    floor = np.where(cnt > 0, 0.0, -BIG).astype(f32)
    small = np.concatenate([
        np.broadcast_to(floor[:, None, :], (P, 8, NT)).reshape(P, 32), cnt,
        (p < 48).astype(f32)[:, None], ((p >= 48) & (p < 96)).astype(f32)[:, None],
        (p[:, None] + P * np.arange(NT)).astype(f32),
        np.broadcast_to(np.arange(NEXP), (P, NEXP)).astype(f32),
        np.broadcast_to(np.arange(NEXP) * CAP - 1, (P, NEXP)).astype(f32),
        q_mask.reshape(P, 16),
        (TOKENS + p[:, None] + P * np.arange(NT)).astype(f32),
        np.zeros((P, 12), f32)], axis=1)
    arrays = {
        "x": a["L0_attn_hidden_states"],
        "wqT": np.ascontiguousarray(a["L0_attn_Wq"].T), "wkT": np.ascontiguousarray(a["L0_attn_Wk"].T),
        "wvT": np.ascontiguousarray(a["L0_attn_Wv"].T),
        "bqkv": np.stack([a["L0_attn_bq"], a["L0_attn_bk"], a["L0_attn_bv"]]),
        "wg": a["L0_ffn_Wg"], "bg": a["L0_ffn_bg"], "w1": a["L0_ffn_W1"], "w2": a["L0_ffn_W2"], "w3": a["L0_ffn_W3"],
        "c_ident": np.eye(P, dtype=f32), "c_rep": rep, "c_kaux": kaux.reshape(32, NCH * P), "c_qaux": qaux,
        "c_tri": np.triu(np.ones((P, P), f32)), "c_small": np.ascontiguousarray(small),
    }
    nc = bacc.Bacc("TRN2", target_bir_lowering=False, num_devices=1)
    t = {k: nc.dram_tensor(k, v.shape, mybir.dt.from_np(v.dtype), kind="ExternalInput").ap() for k, v in arrays.items()}
    out = nc.dram_tensor("out", (TOKENS + TILE, E), F32, kind="ExternalOutput").ap()
    consts = [t[k] for k in ("c_ident", "c_rep", "c_kaux", "c_qaux", "c_tri", "c_small")]
    layer(nc, t["x"], t["wqT"], t["wkT"], t["wvT"], t["bqkv"], t["wg"], t["bg"], t["w1"], t["w2"], t["w3"], consts, out)
    r = run(nc, [arrays], core_ids=[0])
    return r.results[0]["out"][:TOKENS].reshape(NB, S, E)
```
